# Optimizing a Trainium2 kernel written in Bass

```python
import numpy as np
import jax
import jax.numpy as jnp

def _softmax(x, axis=-1):
    return jax.nn.softmax(x, axis=axis)

def _gelu(x):
    return jax.nn.gelu(x, approximate=True)

def _silu(x):
    return jax.nn.silu(x)

def _sigmoid(x):
    return jax.nn.sigmoid(x)

def _layernorm(x, axis=-1, eps=1e-05):
    m = jnp.mean(x, axis=axis, keepdims=True)
    v = jnp.var(x, axis=axis, keepdims=True)
    return (x - m) / jnp.sqrt(v + eps)

def _scatter_add(tgt, idx, src, axis=0):
    return tgt.at[idx].add(src)

def _segment_sum(src, seg, n):
    return jax.ops.segment_sum(src, seg, n)
kernel_name = 'mk_dlrm_tower_d1_rec_r8_8823ed'

def setup_inputs(seed: int=0):
    np.random.seed(seed)
    _w = jnp.asarray

    def _rec_inputs():
        import jax
        import jax.numpy as jnp
        _tk = jax.random.key(seed)
        dense_ctx = jax.random.normal(jax.random.fold_in(_tk, 190), (2048, 16), jnp.float32)
        ids = jnp.stack([jax.random.randint(jax.random.fold_in(_tk, 200 + f), (2048,), 0, v, jnp.int32) for f, v in enumerate([12500, 1000, 1250, 1000, 1000, 12500, 1250, 125000, 125000, 12500, 12500, 1000, 1250, 125000, 1250, 125000, 1250, 125000, 1000, 1250, 1250, 1250, 1250, 1000, 1000, 1250, 12500, 125000, 12500, 125000, 125000, 125000])], axis=1)
        tbl_0 = 0.05 * jax.random.normal(jax.random.fold_in(_tk, 500 + 0), (12500, 16), jnp.float32)
        tbl_1 = 0.05 * jax.random.normal(jax.random.fold_in(_tk, 500 + 1), (1000, 16), jnp.float32)
        tbl_2 = 0.05 * jax.random.normal(jax.random.fold_in(_tk, 500 + 2), (1250, 16), jnp.float32)
        tbl_3 = 0.05 * jax.random.normal(jax.random.fold_in(_tk, 500 + 3), (1000, 16), jnp.float32)
        tbl_4 = 0.05 * jax.random.normal(jax.random.fold_in(_tk, 500 + 4), (1000, 16), jnp.float32)
        tbl_5 = 0.05 * jax.random.normal(jax.random.fold_in(_tk, 500 + 5), (12500, 16), jnp.float32)
        tbl_6 = 0.05 * jax.random.normal(jax.random.fold_in(_tk, 500 + 6), (1250, 16), jnp.float32)
        tbl_7 = 0.05 * jax.random.normal(jax.random.fold_in(_tk, 500 + 7), (125000, 16), jnp.float32)
        tbl_8 = 0.05 * jax.random.normal(jax.random.fold_in(_tk, 500 + 8), (125000, 16), jnp.float32)
        tbl_9 = 0.05 * jax.random.normal(jax.random.fold_in(_tk, 500 + 9), (12500, 16), jnp.float32)
        tbl_10 = 0.05 * jax.random.normal(jax.random.fold_in(_tk, 500 + 10), (12500, 16), jnp.float32)
        tbl_11 = 0.05 * jax.random.normal(jax.random.fold_in(_tk, 500 + 11), (1000, 16), jnp.float32)
        tbl_12 = 0.05 * jax.random.normal(jax.random.fold_in(_tk, 500 + 12), (1250, 16), jnp.float32)
        tbl_13 = 0.05 * jax.random.normal(jax.random.fold_in(_tk, 500 + 13), (125000, 16), jnp.float32)
        tbl_14 = 0.05 * jax.random.normal(jax.random.fold_in(_tk, 500 + 14), (1250, 16), jnp.float32)
        tbl_15 = 0.05 * jax.random.normal(jax.random.fold_in(_tk, 500 + 15), (125000, 16), jnp.float32)
        tbl_16 = 0.05 * jax.random.normal(jax.random.fold_in(_tk, 500 + 16), (1250, 16), jnp.float32)
        tbl_17 = 0.05 * jax.random.normal(jax.random.fold_in(_tk, 500 + 17), (125000, 16), jnp.float32)
        tbl_18 = 0.05 * jax.random.normal(jax.random.fold_in(_tk, 500 + 18), (1000, 16), jnp.float32)
        tbl_19 = 0.05 * jax.random.normal(jax.random.fold_in(_tk, 500 + 19), (1250, 16), jnp.float32)
        tbl_20 = 0.05 * jax.random.normal(jax.random.fold_in(_tk, 500 + 20), (1250, 16), jnp.float32)
        tbl_21 = 0.05 * jax.random.normal(jax.random.fold_in(_tk, 500 + 21), (1250, 16), jnp.float32)
        tbl_22 = 0.05 * jax.random.normal(jax.random.fold_in(_tk, 500 + 22), (1250, 16), jnp.float32)
        tbl_23 = 0.05 * jax.random.normal(jax.random.fold_in(_tk, 500 + 23), (1000, 16), jnp.float32)
        tbl_24 = 0.05 * jax.random.normal(jax.random.fold_in(_tk, 500 + 24), (1000, 16), jnp.float32)
        tbl_25 = 0.05 * jax.random.normal(jax.random.fold_in(_tk, 500 + 25), (1250, 16), jnp.float32)
        tbl_26 = 0.05 * jax.random.normal(jax.random.fold_in(_tk, 500 + 26), (12500, 16), jnp.float32)
        tbl_27 = 0.05 * jax.random.normal(jax.random.fold_in(_tk, 500 + 27), (125000, 16), jnp.float32)
        tbl_28 = 0.05 * jax.random.normal(jax.random.fold_in(_tk, 500 + 28), (12500, 16), jnp.float32)
        tbl_29 = 0.05 * jax.random.normal(jax.random.fold_in(_tk, 500 + 29), (125000, 16), jnp.float32)
        tbl_30 = 0.05 * jax.random.normal(jax.random.fold_in(_tk, 500 + 30), (125000, 16), jnp.float32)
        tbl_31 = 0.05 * jax.random.normal(jax.random.fold_in(_tk, 500 + 31), (125000, 16), jnp.float32)
        _rk = jax.random.fold_in(_tk, 7)
        W_top1 = 0.0441942 * jax.random.normal(jax.random.fold_in(_tk, 801), (512, 512), jnp.float32)
        W_top2 = 0.0441942 * jax.random.normal(jax.random.fold_in(_tk, 802), (512, 256), jnp.float32)
        W_top3 = 0.0625 * jax.random.normal(jax.random.fold_in(_tk, 803), (256, 1), jnp.float32)
        b_top1 = jnp.zeros((512,), jnp.float32)
        b_top2 = jnp.zeros((256,), jnp.float32)
        return (dense_ctx, ids, tbl_0, tbl_1, tbl_2, tbl_3, tbl_4, tbl_5, tbl_6, tbl_7, tbl_8, tbl_9, tbl_10, tbl_11, tbl_12, tbl_13, tbl_14, tbl_15, tbl_16, tbl_17, tbl_18, tbl_19, tbl_20, tbl_21, tbl_22, tbl_23, tbl_24, tbl_25, tbl_26, tbl_27, tbl_28, tbl_29, tbl_30, tbl_31, W_top1, b_top1, W_top2, b_top2, W_top3)
    dense_ctx, ids, tbl_0, tbl_1, tbl_2, tbl_3, tbl_4, tbl_5, tbl_6, tbl_7, tbl_8, tbl_9, tbl_10, tbl_11, tbl_12, tbl_13, tbl_14, tbl_15, tbl_16, tbl_17, tbl_18, tbl_19, tbl_20, tbl_21, tbl_22, tbl_23, tbl_24, tbl_25, tbl_26, tbl_27, tbl_28, tbl_29, tbl_30, tbl_31, W_top1, b_top1, W_top2, b_top2, W_top3 = _rec_inputs()

    def _L0_rec_setup():
        import jax, jax.numpy as jnp
        import numpy as np

        def _pair_indices(num_fields: int):
            row, col = ([], [])
            for i in range(num_fields - 1):
                for j in range(i + 1, num_fields):
                    row.append(i)
                    col.append(j)
            return (np.asarray(row, dtype=np.int32), np.asarray(col, dtype=np.int32))
        key = jax.random.key(seed)
        B, F, D = (2048, 32, 16)
        x = jax.random.normal(key, (B, F, D), dtype=jnp.float32)
        return {'x': x}
    _L0_rec_all = _L0_rec_setup()
    _L0_rec_in = {k: v for k, v in _L0_rec_all.items() if k in ()}
    del _L0_rec_all
    return {'dense_ctx': dense_ctx, 'ids': ids, 'tbl_0': tbl_0, 'tbl_1': tbl_1, 'tbl_2': tbl_2, 'tbl_3': tbl_3, 'tbl_4': tbl_4, 'tbl_5': tbl_5, 'tbl_6': tbl_6, 'tbl_7': tbl_7, 'tbl_8': tbl_8, 'tbl_9': tbl_9, 'tbl_10': tbl_10, 'tbl_11': tbl_11, 'tbl_12': tbl_12, 'tbl_13': tbl_13, 'tbl_14': tbl_14, 'tbl_15': tbl_15, 'tbl_16': tbl_16, 'tbl_17': tbl_17, 'tbl_18': tbl_18, 'tbl_19': tbl_19, 'tbl_20': tbl_20, 'tbl_21': tbl_21, 'tbl_22': tbl_22, 'tbl_23': tbl_23, 'tbl_24': tbl_24, 'tbl_25': tbl_25, 'tbl_26': tbl_26, 'tbl_27': tbl_27, 'tbl_28': tbl_28, 'tbl_29': tbl_29, 'tbl_30': tbl_30, 'tbl_31': tbl_31, 'W_top1': W_top1, 'b_top1': b_top1, 'W_top2': W_top2, 'b_top2': b_top2, 'W_top3': W_top3}

def reference(dense_ctx, ids, tbl_0, tbl_1, tbl_2, tbl_3, tbl_4, tbl_5, tbl_6, tbl_7, tbl_8, tbl_9, tbl_10, tbl_11, tbl_12, tbl_13, tbl_14, tbl_15, tbl_16, tbl_17, tbl_18, tbl_19, tbl_20, tbl_21, tbl_22, tbl_23, tbl_24, tbl_25, tbl_26, tbl_27, tbl_28, tbl_29, tbl_30, tbl_31, W_top1, b_top1, W_top2, b_top2, W_top3):
    import jax
    import jax.numpy as jnp

    def _L0_rec_ref(x):
        import jax, jax.numpy as jnp
        import numpy as np

        def _pair_indices(num_fields: int):
            row, col = ([], [])
            for i in range(num_fields - 1):
                for j in range(i + 1, num_fields):
                    row.append(i)
                    col.append(j)
            return (np.asarray(row, dtype=np.int32), np.asarray(col, dtype=np.int32))
        num_fields = x.shape[1]
        row, col = _pair_indices(num_fields)
        return jnp.sum(x[:, row, :] * x[:, col, :], axis=2)
    e = jnp.stack([tbl_0[ids[:, 0]], tbl_1[ids[:, 1]], tbl_2[ids[:, 2]], tbl_3[ids[:, 3]], tbl_4[ids[:, 4]], tbl_5[ids[:, 5]], tbl_6[ids[:, 6]], tbl_7[ids[:, 7]], tbl_8[ids[:, 8]], tbl_9[ids[:, 9]], tbl_10[ids[:, 10]], tbl_11[ids[:, 11]], tbl_12[ids[:, 12]], tbl_13[ids[:, 13]], tbl_14[ids[:, 14]], tbl_15[ids[:, 15]], tbl_16[ids[:, 16]], tbl_17[ids[:, 17]], tbl_18[ids[:, 18]], tbl_19[ids[:, 19]], tbl_20[ids[:, 20]], tbl_21[ids[:, 21]], tbl_22[ids[:, 22]], tbl_23[ids[:, 23]], tbl_24[ids[:, 24]], tbl_25[ids[:, 25]], tbl_26[ids[:, 26]], tbl_27[ids[:, 27]], tbl_28[ids[:, 28]], tbl_29[ids[:, 29]], tbl_30[ids[:, 30]], tbl_31[ids[:, 31]]], axis=1)
    z = _L0_rec_ref(e)
    z = z.reshape(z.shape[0], -1)
    h = jnp.concatenate([z, dense_ctx], axis=1)
    h = jnp.maximum(h @ W_top1 + b_top1, 0.0)
    h = jnp.maximum(h @ W_top2 + b_top2, 0.0)
    y = h @ W_top3
    return y

_drawn_inputs = setup_inputs


def setup_inputs(seed=0):
    import zlib

    import numpy as np

    out = dict(_drawn_inputs(seed))
    spreads = {'b_top1': (0.0, 0.1), 'b_top2': (0.0, 0.1)}
    factors = {'tbl_0': 5.13,
     'tbl_1': 4.794,
     'tbl_2': 4.543,
     'tbl_3': 4.594,
     'tbl_4': 3.864,
     'tbl_5': 4.949,
     'tbl_6': 4.526,
     'tbl_7': 4.033,
     'tbl_8': 4.548,
     'tbl_9': 4.489,
     'tbl_10': 4.592,
     'tbl_11': 4.315,
     'tbl_12': 4.014,
     'tbl_13': 4.257,
     'tbl_14': 4.562,
     'tbl_15': 4.513,
     'tbl_16': 4.159,
     'tbl_17': 4.793,
     'tbl_18': 4.109,
     'tbl_19': 4.501,
     'tbl_20': 4.148,
     'tbl_21': 4.351,
     'tbl_22': 4.544,
     'tbl_23': 4.689,
     'tbl_24': 4.824,
     'tbl_25': 4.17,
     'tbl_26': 4.571,
     'tbl_27': 4.422,
     'tbl_28': 4.644,
     'tbl_29': 4.452,
     'tbl_30': 4.512,
     'tbl_31': 5.047}
    for name, (base, spread) in spreads.items():
        noise = np.random.default_rng([zlib.crc32(name.encode()), seed]).standard_normal(out[name].shape)
        drawn = base * np.exp(spread * noise) if base else spread * noise
        out[name] = jnp.asarray(drawn.astype(out[name].dtype))
    for name, factor in factors.items():
        out[name] = (out[name] * factor).astype(out[name].dtype)
    return out
```

```python
from contextlib import ExitStack

import concourse.bass as bass
from concourse import mybir

P = 128
B, F, D = 2048, 32, 16
N_DENSE, H1, H2 = 16, 512, 256
N_PAIRS = F * (F - 1) // 2
TILES = B // P
SLOTS = 8
WRAP = F // 2
CHUNK = P // F
CHUNKS = (N_PAIRS + N_DENSE) // P
LAST = N_PAIRS - (CHUNKS - 1) * P
GROUP = 2
GROUPS = TILES // GROUP
GB = GROUP * P

F32 = mybir.dt.float32
I32 = mybir.dt.int32
ALU = mybir.AluOpType
ACT = mybir.ActivationFunctionType
AX = mybir.AxisListType

FIELDS = list(range(F))


def mlp_input_rows():
    rows = []
    for k in range(1, F // 2 + 1):
        for i in range(F if k < F // 2 else F // 2):
            a, b = sorted((FIELDS[i], FIELDS[(i + k) % F]))
            rows.append(a * (2 * F - a - 1) // 2 + b - a - 1)
    return rows + list(range(N_PAIRS, N_PAIRS + N_DENSE))


def dlrm_tower(nc, dense, ids, w1_rows, tables, w1, b1, w2, b2, w3, out):
    with ExitStack() as ctx:
        def sb(name, shape, dt=F32):
            return ctx.enter_context(nc.sbuf_tensor(name, shape, dt))

        def sem(name):
            return ctx.enter_context(nc.semaphore(name))

        emb = sb("emb", [P, SLOTS, (F + WRAP) * D])
        idx = sb("idx", [P, TILES, F], I32)
        prod = sb("prod", [P, CHUNKS, P * D])
        z_last = sb("z_last", [P, 2, P])
        zT = sb("zT", [P, 2, CHUNKS, GB])
        h1T = sb("h1T", [P, H1 // P, GB])
        h2T = sb("h2T", [P, H2 // P, GB])
        y = sb("y", [1, B])
        w1_sb = sb("w1_sb", [P, CHUNKS, H1])
        w2_sb = sb("w2_sb", [P, H1 // P, H2])
        w3_sb = sb("w3_sb", [P, H2 // P])
        b1_sb = sb("b1_sb", [P, H1 // P])
        b2_sb = sb("b2_sb", [P, H2 // P])
        rows_sb = sb("rows_sb", [P, CHUNKS], I32)
        ident = sb("ident", [P, P])
        bank = ctx.enter_context(nc.psum_tensor("bank", [P, 8, 512], F32))
        Z_BANK, H1_BANK, H2_BANK, Y_BANK = 0, 2, 4, 6

        ids_loaded = sem("ids_loaded")
        rows_loaded = sem("rows_loaded")
        w1_loaded = sem("w1_loaded")
        w_loaded = sem("w_loaded")
        dense_loaded = [sem(f"dense_loaded{i}") for i in range(2)]
        ident_zeroed = sem("ident_zeroed")
        ident_ready = sem("ident_ready")
        gathered = [sem(f"gathered{i}") for i in range(SLOTS)]
        wrapped = sem("wrapped")
        prod_ready = sem("prod_ready")
        turned = sem("turned")
        last_prod = sem("last_prod")
        z_last_ready = sem("z_last_ready")
        z_copied = sem("z_copied")
        h1_ready = sem("h1_ready")
        h1_done = sem("h1_done")
        h2_ready = sem("h2_ready")
        h2_done = sem("h2_done")
        y_ready = sem("y_ready")
        y_copied = sem("y_copied")
        stored = sem("stored")

        dense_v = dense.rearrange("(t p) m -> p t m", p=P)

        def tile_turned(t):
            return (CHUNKS - 1) * (t + 2)

        block = ctx.enter_context(nc.Block())

        @block.sync
        def _(sp):
            sp.dma_start(idx[:], ids.rearrange("(t p) f -> p t f", p=P)).then_inc(ids_loaded, 16)
            sp.dma_start(rows_sb[:], w1_rows).then_inc(rows_loaded, 16)
            for t in range(2):
                sp.dma_start(z_last[:, t, LAST:P], dense_v[:, t, :]).then_inc(dense_loaded[t], 16)
            sp.dma_start(w2_sb[:], w2.rearrange("(c p) n -> p c n", p=P)).then_inc(w_loaded, 16)
            sp.dma_start(w3_sb[:], w3).then_inc(w_loaded, 16)
            sp.dma_start(b1_sb[:], b1).then_inc(w_loaded, 16)
            sp.dma_start(b2_sb[:], b2).then_inc(w_loaded, 16)
            with sp.Fori(1, TILES // 2) as j:
                for s in range(2):
                    sp.wait_ge(turned, tile_turned(2 * j + s - 2))
                    sp.dma_start(z_last[:, s, LAST:P], dense_v[:, bass.ds(2 * j + s, 1), :]
                                 ).then_inc(dense_loaded[s], 16)
            sp.wait_ge(y_copied, GROUPS)
            sp.dma_start(out.rearrange("b o -> o b"), y[:]).then_inc(stored, 16)
            sp.wait_ge(stored, 16)

        @block.gpsimd
        def _(pool):
            nc.gpsimd.memset(ident[:], 0.0).then_inc(ident_zeroed, 1)
            pool.wait_ge(ident_zeroed, 1)
            nc.gpsimd.affine_select(out=ident[:], in_=ident[:], compare_op=ALU.not_equal, fill=1.0, base=0,
                                    pattern=[[-1, P]], channel_multiplier=1).then_inc(ident_ready, 1)
            pool.wait_ge(ids_loaded, 16)

            def gather(t, s):
                if t >= SLOTS:
                    pool.wait_ge(prod_ready, 3 * (t - SLOTS + 1))
                for pos, f in enumerate(FIELDS):
                    nc.gpsimd.indirect_dma_start(
                        emb[:, s, pos * D:(pos + 1) * D], None, tables[f],
                        bass.IndirectOffsetOnAxis(ap=idx[:, t, f:f + 1], axis=0)).then_inc(gathered[s], 16)

            for t in range(TILES):
                gather(t, t % SLOTS)
                if t == 0:
                    pool.wait_ge(rows_loaded, 16)
                    for c in range(CHUNKS):
                        nc.gpsimd.indirect_dma_start(
                            w1_sb[:, c, :], None, w1,
                            bass.IndirectOffsetOnAxis(ap=rows_sb[:, c:c + 1], axis=0)).then_inc(w1_loaded, 16)

        @block.vector
        def _(dve):
            nc.vector.memset(y[:, 1:2], 0.0).then_inc(turned, CHUNKS - 1)
            nc.vector.memset(y[:, 2:3], 0.0).then_inc(z_copied, 2)
            nc.vector.memset(y[:, 3:4], 0.0).then_inc(h1_done, 2)

            def products(s, c):
                k0 = 1 + c * CHUNK
                ks = CHUNK if c < CHUNKS - 1 else CHUNK - 1
                e = emb[:, s, 0:F * D].unsqueeze(1).to_broadcast([P, ks, F * D])
                e2 = windows(s, k0, ks)
                return nc.vector.tensor_tensor(
                    prod[:, c, 0:ks * F * D].rearrange("p (k x) -> p k x", k=ks), e, e2, ALU.mult)

            def windows(s, k0, ks):
                w = emb[:, s, k0 * D:k0 * D + F * D]
                w = w.unsqueeze(1).to_broadcast([P, ks, F * D])
                ap = [list(x) for x in w.ap]
                ap[1][0] = D
                return bass.AP(tensor=w.tensor, offset=w.offset, ap=ap)

            with dve.Fori(0, TILES // SLOTS) as half:
                for s in range(SLOTS):
                    t = half * SLOTS + s
                    dve.wait_ge(gathered[s], (half + 1) * 16 * F)
                    nc.vector.tensor_copy(emb[:, s, F * D:], emb[:, s, 0:WRAP * D]).then_inc(wrapped, 1)
                    dve.wait_ge(wrapped, t + 1)
                    products(s, CHUNKS - 1)
                    half_way = (CHUNK - 1) * F * D
                    nc.vector.tensor_tensor(prod[:, CHUNKS - 1, half_way:LAST * D], emb[:, s, 0:F * D // 2],
                                            emb[:, s, F * D // 2:F * D], ALU.mult).then_inc(last_prod, 1)
                    dve.wait_ge(turned, 3 * t + 1)
                    products(s, 0).then_inc(prod_ready, 1)
                    dve.wait_ge(last_prod, t + 1)
                    nc.vector.tensor_reduce(z_last[:, s % 2, 0:LAST],
                                            prod[:, CHUNKS - 1, 0:LAST * D].rearrange("p (a d) -> p a d", d=D),
                                            AX.X, ALU.add).then_inc(z_last_ready, 1)
                    dve.wait_ge(turned, 3 * t + 2)
                    products(s, 1).then_inc(prod_ready, 1)
                    dve.wait_ge(turned, 3 * t + 3)
                    products(s, 2).then_inc(prod_ready, 1)

        @block.tensor
        def _(pe):
            def sum_chunk(t, s, c):
                pe.wait_ge(prod_ready, 3 * t + c + 1)
                v = prod[:, c, :].rearrange("p (a d) -> p d a", d=D)
                for d in range(D):
                    mm = nc.tensor.matmul(bank[:, Z_BANK + s % 2, c * P:(c + 1) * P], v[:, d, :], ident[:],
                                          start=(d == 0), stop=(d == D - 1), is_transpose=True)
                mm.then_inc(turned, 1)

            def turn_last(t, s):
                pe.wait_ge(z_last_ready, t + 1)
                pe.wait_ge(dense_loaded[s % 2], (t - s % 2) * 8 + 16)
                c = CHUNKS - 1
                nc.tensor.matmul(bank[:, Z_BANK + s % 2, c * P:(c + 1) * P], z_last[:, s % 2, :], ident[:],
                                 start=True, stop=True, is_transpose=True)

            def layer1(g, half, n):
                pe.wait_ge(h1_done, 4 * g + n + 1)
                for c in range(CHUNKS):
                    mm = nc.tensor.matmul(bank[:, H1_BANK + n % 2, 0:GB], w1_sb[:, c, n * P:(n + 1) * P],
                                          zT[:, half, c, :], start=(c == 0), stop=(c == CHUNKS - 1))
                mm.then_inc(h1_ready, 1)

            def layer2(g, m):
                if m == 0:
                    pe.wait_ge(h1_done, 4 * g + 4 + 2)
                for c in range(H1 // P):
                    mm = nc.tensor.matmul(bank[:, H2_BANK + m, 0:GB], w2_sb[:, c, m * P:(m + 1) * P],
                                          h1T[:, c, :], start=(c == 0), stop=(c == H1 // P - 1))
                mm.then_inc(h2_ready, 1)

            def layer3(g):
                pe.wait_ge(h2_done, 2 * g + 2)
                for c in range(H2 // P):
                    mm = nc.tensor.matmul(bank[0:1, Y_BANK, 0:GB], w3_sb[:, c:c + 1],
                                          h2T[:, c, :], start=(c == 0), stop=(c == H2 // P - 1))
                mm.then_inc(y_ready, 1)

            def group(g, half, mlp):
                prev = 1 - half
                t = 2 * g
                pe.wait_ge(z_copied, t + 1)
                sum_chunk(t, 0, 0)
                if mlp:
                    pe.wait_ge(z_copied, t + 2)
                    layer1(g - 1, prev, 0)
                turn_last(t, 0)
                sum_chunk(t, 0, 1)
                if mlp:
                    layer1(g - 1, prev, 1)
                sum_chunk(t, 0, 2)
                if mlp:
                    layer1(g - 1, prev, 2)
                pe.wait_ge(z_copied, t + 2)
                sum_chunk(t + 1, 1, 0)
                if mlp:
                    layer1(g - 1, prev, 3)
                turn_last(t + 1, 1)
                sum_chunk(t + 1, 1, 1)
                if mlp:
                    layer2(g - 1, 0)
                    layer2(g - 1, 1)
                sum_chunk(t + 1, 1, 2)
                if mlp:
                    layer3(g - 1)

            pe.wait_ge(ident_ready, 1)
            group(0, 0, False)
            pe.wait_ge(w1_loaded, 16 * CHUNKS)
            pe.wait_ge(w_loaded, 64)
            with pe.Fori(0, GROUPS // 2 - 1) as j:
                group(2 * j + 1, 1, True)
                group(2 * j + 2, 0, True)
            group(GROUPS - 1, 1, True)
            pe.wait_ge(z_copied, TILES + 2)
            for n in range(4):
                layer1(GROUPS - 1, 1, n)
            for m in range(2):
                layer2(GROUPS - 1, m)
            layer3(GROUPS - 1)

        @block.scalar
        def _(act):
            def copy_z(t, half, s):
                act.wait_ge(turned, tile_turned(t))
                nc.scalar.copy(zT[:, half, :, s * P:(s + 1) * P],
                               bank[:, Z_BANK + s, :].rearrange("p (c b) -> p c b", c=CHUNKS)
                               ).then_inc(z_copied, 1)

            def relu1(g, n):
                act.wait_ge(h1_ready, 4 * g + n + 1)
                nc.scalar.activation(h1T[:, n, :], bank[:, H1_BANK + n % 2, 0:GB], ACT.Relu,
                                     bias=b1_sb[:, n:n + 1]).then_inc(h1_done, 1)

            def relu2(g, m):
                act.wait_ge(h2_ready, 2 * g + m + 1)
                nc.scalar.activation(h2T[:, m, :], bank[:, H2_BANK + m, 0:GB], ACT.Relu,
                                     bias=b2_sb[:, m:m + 1]).then_inc(h2_done, 1)

            def copy_y(g):
                act.wait_ge(y_ready, g + 1)
                nc.scalar.copy(y[0:1, bass.ts(g, GB)], bank[0:1, Y_BANK, 0:GB]).then_inc(y_copied, 1)

            def group(g, half):
                relu1(g - 1, 0)
                relu1(g - 1, 1)
                copy_z(2 * g, half, 0)
                relu1(g - 1, 2)
                relu1(g - 1, 3)
                relu2(g - 1, 0)
                relu2(g - 1, 1)
                copy_z(2 * g + 1, half, 1)
                copy_y(g - 1)

            act.wait_ge(w_loaded, 64)
            copy_z(0, 0, 0)
            copy_z(1, 0, 1)
            with act.Fori(0, GROUPS // 2 - 1) as j:
                group(2 * j + 1, 1)
                group(2 * j + 2, 0)
            group(GROUPS - 1, 1)
            for n in range(4):
                relu1(GROUPS - 1, n)
            for m in range(2):
                relu2(GROUPS - 1, m)
            copy_y(GROUPS - 1)


def kernel(**inputs):
    import numpy as np
    import concourse.bacc as bacc
    from concourse.bass_utils import run_bass_kernel_spmd

    nc = bacc.Bacc("TRN2", target_bir_lowering=False, num_devices=1)
    arrays = {}

    def given(name, a):
        a = np.ascontiguousarray(a)
        arrays[name] = a
        return nc.dram_tensor(name, a.shape, mybir.dt.from_np(a.dtype), kind="ExternalInput").ap()

    rows = np.array(mlp_input_rows(), np.int32).reshape(CHUNKS, P).T
    tables = [given(f"tbl_{f}", inputs[f"tbl_{f}"]) for f in range(F)]
    args = dict(dense=given("dense", inputs["dense_ctx"]), ids=given("ids", inputs["ids"]),
                w1_rows=given("w1_rows", rows), tables=tables)
    for short, name in (("w1", "W_top1"), ("w2", "W_top2")):
        args[short] = given(short, inputs[name])
    for short, name in (("b1", "b_top1"), ("b2", "b_top2"), ("w3", "W_top3")):
        args[short] = given(short, np.asarray(inputs[name]).reshape(-1, P).T)
    out = nc.dram_tensor("y_out", (B, 1), F32, kind="ExternalOutput").ap()
    dlrm_tower(nc, out=out, **args)
    r = run_bass_kernel_spmd(nc, [arrays], core_ids=[0])
    return r.results[0]["y_out"]
```

```python
from contextlib import ExitStack

import concourse.bass as bass
from concourse import mybir

P = 128
B, F, D = 2048, 32, 16
N_DENSE, H1, H2 = 16, 512, 256
N_PAIRS = F * (F - 1) // 2
TILES = B // P
SLOTS = 8
WRAP = F // 2
CHUNK = P // F
CHUNKS = (N_PAIRS + N_DENSE) // P
LAST = N_PAIRS - (CHUNKS - 1) * P
GROUP = 2
GROUPS = TILES // GROUP
GB = GROUP * P

F32 = mybir.dt.float32
BF16 = mybir.dt.bfloat16
F16 = mybir.dt.float16
I32 = mybir.dt.int32
ALU = mybir.AluOpType
ACT = mybir.ActivationFunctionType
AX = mybir.AxisListType

VOCABS = [12500, 1000, 1250, 1000, 1000, 12500, 1250, 125000, 125000, 12500, 12500, 1000, 1250, 125000, 1250, 125000,
          1250, 125000, 1000, 1250, 1250, 1250, 1250, 1000, 1000, 1250, 12500, 125000, 12500, 125000, 125000, 125000]
SMALL = sorted(sorted(range(F), key=lambda f: VOCABS[f])[:WRAP], key=lambda f: -VOCABS[f])
LARGE = [f for f in range(F) if f not in SMALL]
FIELDS = SMALL + LARGE
SLICES = 10
ROWS = max(VOCABS[f] for f in SMALL) // SLICES
SHORT = sum(VOCABS[f] < ROWS * SLICES for f in SMALL)
PAIRS = len(SMALL) // 2
PARTS = 3
HALF = 64
RING = 5


def mlp_input_rows():
    rows = []
    for k in range(1, F // 2 + 1):
        for i in range(F if k < F // 2 else F // 2):
            a, b = sorted((FIELDS[i], FIELDS[(i + k) % F]))
            rows.append(a * (2 * F - a - 1) // 2 + b - a - 1)
    return rows + list(range(N_PAIRS, N_PAIRS + N_DENSE))


def dlrm_tower(nc, dense, ids, small_ids, w1_rows, tables, w1, b1, w2, b2, w3, out):
    with ExitStack() as ctx:
        def sb(name, shape, dt=F32):
            return ctx.enter_context(nc.sbuf_tensor(name, shape, dt))

        def sem(name):
            return ctx.enter_context(nc.semaphore(name))

        emb = sb("emb", [P, SLOTS, (F + WRAP) * D])
        idx = sb("idx", [P, TILES, F], I32)
        small_emb = sb("small_emb", [P, TILES, WRAP * D])
        tab = sb("tab", [ROWS, 2 * PAIRS, SLICES, D])
        parts = sb("parts", [ROWS, 2, 2, SLICES, HALF], BF16)
        row_of = sb("row_of", [ROWS, SLICES])
        row_of_int = sb("row_of_int", [ROWS, SLICES], I32)
        ids_int = sb("ids_int", [P, 2, B], I32)
        ids_half = sb("ids_half", [P, 2, 2, B], F16)
        onehot = sb("onehot", [ROWS, RING, 2, B], BF16)
        looked_up = sb("looked_up", [P, B], BF16)
        add_parts = sb("add_parts", [P, 2 * D], BF16)
        prod = sb("prod", [P, CHUNKS, P * D])
        z_last = sb("z_last", [P, 2, P])
        zT = sb("zT", [P, 2, CHUNKS, GB])
        h1T = sb("h1T", [P, H1 // P, GB])
        h2T = sb("h2T", [P, H2 // P, GB])
        y = sb("y", [1, B])
        w1_sb = sb("w1_sb", [P, CHUNKS, H1])
        w2_sb = sb("w2_sb", [P, H1 // P, H2])
        w3_sb = sb("w3_sb", [P, H2 // P])
        b1_sb = sb("b1_sb", [P, H1 // P])
        b2_sb = sb("b2_sb", [P, H2 // P])
        rows_sb = sb("rows_sb", [P, CHUNKS], I32)
        ident = sb("ident", [P, P])
        bank = ctx.enter_context(nc.psum_tensor("bank", [P, 8, 512], F32))
        Z_BANK, H1_BANK, H2_BANK, Y_BANK = 0, 2, 4, 6
        LOOK_BANK, SMALL_BANK = 2, 7

        ids_loaded = sem("ids_loaded")
        rows_loaded = sem("rows_loaded")
        w1_loaded = sem("w1_loaded")
        w_loaded = sem("w_loaded")
        dense_loaded = [sem(f"dense_loaded{i}") for i in range(2)]
        ident_zeroed = sem("ident_zeroed")
        ident_ready = sem("ident_ready")
        row_of_made = sem("row_of_made")
        row_of_ready = sem("row_of_ready")
        add_parts_steps = sem("add_parts_steps")
        tab_cleared = sem("tab_cleared")
        parts_cleared = sem("parts_cleared")
        tab_loaded = [sem(f"tab_loaded{i}") for i in range(2)]
        small_ids_loaded = [sem(f"small_ids_loaded{i}") for i in range(2)]
        ids_converted = sem("ids_converted")
        first_part = sem("first_part")
        second_part = sem("second_part")
        rests = sem("rests")
        onehot_made = sem("onehot_made")
        onehot_used = sem("onehot_used")
        look_copied = sem("look_copied")
        parts_added = sem("parts_added")
        small_copied = sem("small_copied")
        small_placed = sem("small_placed")
        gathered = [sem(f"gathered{i}") for i in range(SLOTS)]
        prod_ready = sem("prod_ready")
        turned = sem("turned")
        last_prod = sem("last_prod")
        z_last_ready = sem("z_last_ready")
        z_copied = sem("z_copied")
        h1_ready = sem("h1_ready")
        h1_done = sem("h1_done")
        h2_ready = sem("h2_ready")
        h2_done = sem("h2_done")
        y_ready = sem("y_ready")
        y_copied = sem("y_copied")
        stored = sem("stored")

        dense_v = dense.rearrange("(t p) m -> p t m", p=P)

        def tile_turned(t):
            return (CHUNKS - 1) * (t + 2)

        block = ctx.enter_context(nc.Block())

        @block.sync
        def _(sp):
            sp.dma_start(idx[:], ids.rearrange("(t p) f -> p t f", p=P)).then_inc(ids_loaded, 16)

            def load_table(i, loaded):
                rows = VOCABS[SMALL[i]] // SLICES
                sp.dma_start(tab[0:rows, i, :, :].rearrange("p c d -> p (c d)"),
                             tables[SMALL[i]].rearrange("(p c) d -> p (c d)", c=SLICES)).then_inc(loaded, 16)

            def load_small_ids(i, slot):
                sp.dma_start(ids_int[:, slot, :], small_ids[bass.ds(i, 1), :].to_broadcast([P, B])
                             ).then_inc(small_ids_loaded[slot], 16)

            for i in range(2):
                load_small_ids(i, i)
                load_table(i, tab_loaded[0])
            for i in range(2, 2 * PAIRS - SHORT):
                load_table(i, tab_loaded[1])
            sp.wait_ge(tab_cleared, 1)
            for i in range(2 * PAIRS - SHORT, 2 * PAIRS):
                load_table(i, tab_loaded[1])
            sp.dma_start(rows_sb[:], w1_rows).then_inc(rows_loaded, 16)
            for t in range(2):
                sp.dma_start(z_last[:, t, LAST:P], dense_v[:, t, :]).then_inc(dense_loaded[t], 16)
            sp.dma_start(w2_sb[:], w2.rearrange("(c p) n -> p c n", p=P)).then_inc(w_loaded, 16)
            sp.dma_start(w3_sb[:], w3).then_inc(w_loaded, 16)
            sp.dma_start(b1_sb[:], b1).then_inc(w_loaded, 16)
            sp.dma_start(b2_sb[:], b2).then_inc(w_loaded, 16)
            with sp.Fori(1, PAIRS) as q:
                for i in range(2):
                    sp.wait_ge(ids_converted, 2 * q + i - 1)
                    load_small_ids(2 * q + i, i)
            with sp.Fori(1, TILES // 2) as j:
                for s in range(2):
                    sp.wait_ge(turned, tile_turned(2 * j + s - 2))
                    sp.dma_start(z_last[:, s, LAST:P], dense_v[:, bass.ds(2 * j + s, 1), :]
                                 ).then_inc(dense_loaded[s], 16)
            sp.wait_ge(y_copied, GROUPS)
            sp.dma_start(out.rearrange("b o -> o b"), y[:]).then_inc(stored, 16)
            sp.wait_ge(stored, 16)

        @block.gpsimd
        def _(pool):
            nc.gpsimd.memset(ident[:], 0.0).then_inc(ident_zeroed, 1)
            pool.wait_ge(ident_zeroed, 1)
            nc.gpsimd.affine_select(out=ident[:], in_=ident[:], compare_op=ALU.not_equal, fill=1.0, base=0,
                                    pattern=[[-1, P]], channel_multiplier=1).then_inc(ident_ready, 1)
            nc.gpsimd.iota(row_of_int[:], pattern=[[1, SLICES]], base=0, channel_multiplier=SLICES).then_inc(row_of_made, 1)
            nc.gpsimd.memset(add_parts[:], 0.0).then_inc(add_parts_steps, 1)
            for k in range(PARTS):
                pool.wait_ge(add_parts_steps, k + 1)
                v = add_parts[:].rearrange("p (t d) -> p t d", t=2)
                nc.gpsimd.affine_select(out=v, in_=v, compare_op=ALU.not_equal, fill=1.0, base=-k * D,
                                        pattern=[[-HALF, 2], [-1, D]], channel_multiplier=1
                                        ).then_inc(add_parts_steps, 1)
            pool.wait_ge(ids_loaded, 16)

            def gather(t, s):
                if t >= SLOTS:
                    pool.wait_ge(prod_ready, 3 * (t - SLOTS + 1))
                for pos, f in enumerate(LARGE, WRAP):
                    nc.gpsimd.indirect_dma_start(
                        emb[:, s, pos * D:(pos + 1) * D], None, tables[f],
                        bass.IndirectOffsetOnAxis(ap=idx[:, t, f:f + 1], axis=0)).then_inc(gathered[s], 16)

            for t in range(TILES):
                gather(t, t % SLOTS)
                if t == 0:
                    pool.wait_ge(rows_loaded, 16)
                    for c in range(CHUNKS):
                        nc.gpsimd.indirect_dma_start(
                            w1_sb[:, c, :], None, w1,
                            bass.IndirectOffsetOnAxis(ap=rows_sb[:, c:c + 1], axis=0)).then_inc(w1_loaded, 16)

        @block.vector
        def _(dve):
            nc.vector.memset(y[:, 1:2], 0.0).then_inc(turned, CHUNKS - 1)
            nc.vector.memset(y[:, 2:3], 0.0).then_inc(z_copied, 2)
            nc.vector.memset(y[:, 3:4], 0.0).then_inc(h1_done, 2)

            nc.vector.memset(y[:, 4:5], 0.0).then_inc(onehot_used, RING)
            short = 2 * PAIRS - SHORT
            nc.vector.memset(tab[P - 32:ROWS, short:, :, :], 0.0).then_inc(tab_cleared, 1)
            nc.vector.memset(parts[:, :, :, :, PARTS * D:], 0.0).then_inc(parts_cleared, 1)
            dve.wait_ge(row_of_made, 1)
            nc.vector.tensor_copy(row_of[:], row_of_int[:]).then_inc(row_of_ready, 1)

            def rest_after_first(q, slot):
                dve.wait_ge(first_part, q + 1)
                t = tab[:, bass.ds(2 * q, 2), :, :]
                nc.vector.tensor_tensor(t, t, parts[:, slot, :, :, 0:D], ALU.subtract).then_inc(rests, 1)

            def third_part(q, slot):
                dve.wait_ge(second_part, q + 1)
                nc.vector.tensor_tensor(parts[:, slot, :, :, 2 * D:3 * D], tab[:, bass.ds(2 * q, 2), :, :],
                                        parts[:, slot, :, :, D:2 * D], ALU.subtract).then_inc(rests, 1)

            def onehots(q, slot, prefetch):
                for c in range(SLICES):
                    dve.wait_ge(onehot_used, SLICES * q + c + 1)
                    for i in range(2):
                        if c == 0:
                            dve.wait_ge(ids_converted, 2 * q + i + 1)
                        nc.vector.tensor_scalar(onehot[:, c % RING, i, :], ids_half[0:ROWS, slot, i, :],
                                                row_of[:, c:c + 1], None, ALU.is_equal).then_inc(onehot_made, 1)
                    if prefetch and c == 3:
                        rest_after_first(q + 1, 1 - slot)
                    if prefetch and c == 7:
                        third_part(q + 1, 1 - slot)

            rest_after_first(0, 0)
            third_part(0, 0)
            dve.wait_ge(row_of_ready, 1)
            with dve.Fori(0, PAIRS // 2 - 1) as j:
                onehots(2 * j, 0, True)
                onehots(2 * j + 1, 1, True)
            onehots(PAIRS - 2, 0, True)
            onehots(PAIRS - 1, 1, False)

            def products(s, c):
                k0 = 1 + c * CHUNK
                ks = CHUNK if c < CHUNKS - 1 else CHUNK - 1
                e = emb[:, s, 0:F * D].unsqueeze(1).to_broadcast([P, ks, F * D])
                e2 = windows(s, k0, ks)
                return nc.vector.tensor_tensor(
                    prod[:, c, 0:ks * F * D].rearrange("p (k x) -> p k x", k=ks), e, e2, ALU.mult)

            def windows(s, k0, ks):
                w = emb[:, s, k0 * D:k0 * D + F * D]
                w = w.unsqueeze(1).to_broadcast([P, ks, F * D])
                ap = [list(x) for x in w.ap]
                ap[1][0] = D
                return bass.AP(tensor=w.tensor, offset=w.offset, ap=ap)

            with dve.Fori(0, TILES // SLOTS) as half:
                for s in range(SLOTS):
                    t = half * SLOTS + s
                    dve.wait_ge(small_placed, t + 1)
                    dve.wait_ge(gathered[s], (half + 1) * 16 * len(LARGE))
                    products(s, CHUNKS - 1)
                    half_way = (CHUNK - 1) * F * D
                    nc.vector.tensor_tensor(prod[:, CHUNKS - 1, half_way:LAST * D], emb[:, s, 0:F * D // 2],
                                            emb[:, s, F * D // 2:F * D], ALU.mult).then_inc(last_prod, 1)
                    dve.wait_ge(turned, 3 * t + 1)
                    products(s, 0).then_inc(prod_ready, 1)
                    dve.wait_ge(last_prod, t + 1)
                    nc.vector.tensor_reduce(z_last[:, s % 2, 0:LAST],
                                            prod[:, CHUNKS - 1, 0:LAST * D].rearrange("p (a d) -> p a d", d=D),
                                            AX.X, ALU.add).then_inc(z_last_ready, 1)
                    dve.wait_ge(turned, 3 * t + 2)
                    products(s, 1).then_inc(prod_ready, 1)
                    dve.wait_ge(turned, 3 * t + 3)
                    products(s, 2).then_inc(prod_ready, 1)
                    dve.wait_ge(z_last_ready, t + 1)

        @block.tensor
        def _(pe):
            def sum_chunk(t, s, c):
                pe.wait_ge(prod_ready, 3 * t + c + 1)
                v = prod[:, c, :].rearrange("p (a d) -> p d a", d=D)
                for d in range(D):
                    mm = nc.tensor.matmul(bank[:, Z_BANK + s % 2, c * P:(c + 1) * P], v[:, d, :], ident[:],
                                          start=(d == 0), stop=(d == D - 1), is_transpose=True)
                mm.then_inc(turned, 1)

            def turn_last(t, s):
                pe.wait_ge(z_last_ready, t + 1)
                pe.wait_ge(dense_loaded[s % 2], (t - s % 2) * 8 + 16)
                c = CHUNKS - 1
                nc.tensor.matmul(bank[:, Z_BANK + s % 2, c * P:(c + 1) * P], z_last[:, s % 2, :], ident[:],
                                 start=True, stop=True, is_transpose=True)

            def layer1(g, half, n):
                pe.wait_ge(h1_done, 4 * g + n + 1)
                for c in range(CHUNKS):
                    mm = nc.tensor.matmul(bank[:, H1_BANK + n % 2, 0:GB], w1_sb[:, c, n * P:(n + 1) * P],
                                          zT[:, half, c, :], start=(c == 0), stop=(c == CHUNKS - 1))
                mm.then_inc(h1_ready, 1)

            def layer2(g, m):
                if m == 0:
                    pe.wait_ge(h1_done, 4 * g + 4 + 2)
                for c in range(H1 // P):
                    mm = nc.tensor.matmul(bank[:, H2_BANK + m, 0:GB], w2_sb[:, c, m * P:(m + 1) * P],
                                          h1T[:, c, :], start=(c == 0), stop=(c == H1 // P - 1))
                mm.then_inc(h2_ready, 1)

            def layer3(g):
                pe.wait_ge(h2_done, 2 * g + 2)
                for c in range(H2 // P):
                    mm = nc.tensor.matmul(bank[0:1, Y_BANK, 0:GB], w3_sb[:, c:c + 1],
                                          h2T[:, c, :], start=(c == 0), stop=(c == H2 // P - 1))
                mm.then_inc(y_ready, 1)

            def group(g, half, mlp):
                prev = 1 - half
                t = 2 * g
                pe.wait_ge(z_copied, t + 1)
                sum_chunk(t, 0, 0)
                if mlp:
                    pe.wait_ge(z_copied, t + 2)
                    layer1(g - 1, prev, 0)
                turn_last(t, 0)
                sum_chunk(t, 0, 1)
                if mlp:
                    layer1(g - 1, prev, 1)
                sum_chunk(t, 0, 2)
                if mlp:
                    layer1(g - 1, prev, 2)
                pe.wait_ge(z_copied, t + 2)
                sum_chunk(t + 1, 1, 0)
                if mlp:
                    layer1(g - 1, prev, 3)
                turn_last(t + 1, 1)
                sum_chunk(t + 1, 1, 1)
                if mlp:
                    layer2(g - 1, 0)
                    layer2(g - 1, 1)
                sum_chunk(t + 1, 1, 2)
                if mlp:
                    layer3(g - 1)

            def look_up(q, slot):
                pe.wait_ge(rests, 2 * q + 2)
                for c in range(SLICES):
                    pe.wait_ge(onehot_made, 2 * (SLICES * q + c) + 2)
                    for g in range(4):
                        for i in range(2):
                            mm = nc.tensor.matmul(bank[i * HALF:(i + 1) * HALF, LOOK_BANK + g, :],
                                                  parts[:, slot, i, c, :],
                                                  onehot[:, c % RING, i, g * 512:(g + 1) * 512],
                                                  start=(c == 0), stop=(c == SLICES - 1))
                    mm.then_inc(onehot_used, 1)

            def whole(q):
                for t in range(TILES):
                    if t % (TILES // 2) == 0:
                        pe.wait_ge(look_copied, 2 * q + 1 + t // (TILES // 2))
                    mm = nc.tensor.matmul(bank[:, SMALL_BANK, t * 2 * D:(t + 1) * 2 * D],
                                          looked_up[:, t * P:(t + 1) * P], add_parts[:], start=True, stop=True)
                mm.then_inc(parts_added, 1)

            pe.wait_ge(parts_cleared, 1)
            pe.wait_ge(add_parts_steps, 1 + PARTS)
            with pe.Fori(0, PAIRS // 2) as j:
                for slot in range(2):
                    look_up(2 * j + slot, slot)
                    whole(2 * j + slot)

            pe.wait_ge(ident_ready, 1)
            group(0, 0, False)
            pe.wait_ge(w1_loaded, 16 * CHUNKS)
            pe.wait_ge(w_loaded, 64)
            with pe.Fori(0, GROUPS // 2 - 1) as j:
                group(2 * j + 1, 1, True)
                group(2 * j + 2, 0, True)
            group(GROUPS - 1, 1, True)
            pe.wait_ge(z_copied, TILES + 2)
            for n in range(4):
                layer1(GROUPS - 1, 1, n)
            for m in range(2):
                layer2(GROUPS - 1, m)
            layer3(GROUPS - 1)

        @block.scalar
        def _(act):
            def copy_z(t, half, s):
                act.wait_ge(turned, tile_turned(t))
                nc.scalar.copy(zT[:, half, :, s * P:(s + 1) * P],
                               bank[:, Z_BANK + s, :].rearrange("p (c b) -> p c b", c=CHUNKS)
                               ).then_inc(z_copied, 1)

            def relu1(g, n):
                act.wait_ge(h1_ready, 4 * g + n + 1)
                nc.scalar.activation(h1T[:, n, :], bank[:, H1_BANK + n % 2, 0:GB], ACT.Relu,
                                     bias=b1_sb[:, n:n + 1]).then_inc(h1_done, 1)

            def relu2(g, m):
                act.wait_ge(h2_ready, 2 * g + m + 1)
                nc.scalar.activation(h2T[:, m, :], bank[:, H2_BANK + m, 0:GB], ACT.Relu,
                                     bias=b2_sb[:, m:m + 1]).then_inc(h2_done, 1)

            def copy_y(g):
                act.wait_ge(y_ready, g + 1)
                nc.scalar.copy(y[0:1, bass.ts(g, GB)], bank[0:1, Y_BANK, 0:GB]).then_inc(y_copied, 1)

            def place_small(t, slot):
                nc.scalar.copy(emb[:, slot, :].rearrange("p (k x) -> p k x", x=WRAP * D)[:, 0:3:2, :],
                               small_emb[:, bass.ds(t, 1), :].to_broadcast([P, 2, WRAP * D])
                               ).then_inc(small_placed, 1)

            def group(g, half, slot):
                if slot is not None:
                    place_small(2 * g + 2, slot)
                    place_small(2 * g + 3, slot + 1)
                relu1(g - 1, 0)
                relu1(g - 1, 1)
                copy_z(2 * g, half, 0)
                relu1(g - 1, 2)
                relu1(g - 1, 3)
                relu2(g - 1, 0)
                relu2(g - 1, 1)
                copy_z(2 * g + 1, half, 1)
                copy_y(g - 1)

            def convert_ids(q, slot, i):
                act.wait_ge(small_ids_loaded[i], 16 * q + 16)
                nc.scalar.copy(ids_half[:, slot, i, :], ids_int[:, i, :]).then_inc(ids_converted, 1)

            def first(q, slot):
                nc.scalar.copy(parts[:, slot, :, :, 0:D], tab[:, bass.ds(2 * q, 2), :, :]).then_inc(first_part, 1)

            def second(q, slot):
                nc.scalar.copy(parts[:, slot, :, :, D:2 * D], tab[:, bass.ds(2 * q, 2), :, :]
                               ).then_inc(second_part, 1)

            def pair(q, slot, more):
                if more:
                    act.wait_ge(onehot_made, 2 * SLICES * q + 1)
                    act.wait_ge(onehot_used, SLICES * q + RING)
                    convert_ids(q + 1, 1 - slot, 0)
                    first(q + 1, 1 - slot)
                    act.wait_ge(rests, 2 * q + 3)
                    convert_ids(q + 1, 1 - slot, 1)
                    second(q + 1, 1 - slot)
                act.wait_ge(onehot_used, SLICES * (q + 1) + RING)
                for h in range(2):
                    nc.scalar.copy(looked_up[:, h * B // 2:(h + 1) * B // 2].rearrange("p (g b) -> p g b", g=2),
                                   bank[:, LOOK_BANK + 2 * h:LOOK_BANK + 2 * h + 2, :]).then_inc(look_copied, 1)
                act.wait_ge(parts_added, q + 1)
                act.nop()
                nc.scalar.copy(small_emb[:, :, bass.ds(2 * D * q, 2 * D)],
                               bank[:, SMALL_BANK, :].rearrange("p (t x) -> p t x", t=TILES)
                               ).then_inc(small_copied, 1)

            act.wait_ge(tab_loaded[0], 32)
            first(0, 0)
            convert_ids(0, 0, 0)
            act.wait_ge(rests, 1)
            second(0, 0)
            convert_ids(0, 0, 1)
            act.wait_ge(tab_loaded[1], 16 * (2 * PAIRS - 2))
            with act.Fori(0, PAIRS // 2 - 1) as j:
                pair(2 * j, 0, True)
                pair(2 * j + 1, 1, True)
            pair(PAIRS - 2, 0, True)
            pair(PAIRS - 1, 1, False)

            act.wait_ge(w_loaded, 64)
            act.wait_ge(small_copied, PAIRS)
            for t in range(4):
                place_small(t, t)
            copy_z(0, 0, 0)
            copy_z(1, 0, 1)
            for g in range(1, GROUPS):
                group(g, g % 2, (2 * g + 2) % SLOTS if g < GROUPS - 1 else None)
            for n in range(4):
                relu1(GROUPS - 1, n)
            for m in range(2):
                relu2(GROUPS - 1, m)
            copy_y(GROUPS - 1)


def kernel(**inputs):
    import numpy as np
    import concourse.bacc as bacc
    from concourse.bass_utils import run_bass_kernel_spmd

    nc = bacc.Bacc("TRN2", target_bir_lowering=False, num_devices=1)
    arrays = {}

    def given(name, a):
        a = np.ascontiguousarray(a)
        arrays[name] = a
        return nc.dram_tensor(name, a.shape, mybir.dt.from_np(a.dtype), kind="ExternalInput").ap()

    rows = np.array(mlp_input_rows(), np.int32).reshape(CHUNKS, P).T
    tables = [given(f"tbl_{f}", inputs[f"tbl_{f}"]) for f in range(F)]
    assert [inputs[f"tbl_{f}"].shape[0] for f in range(F)] == VOCABS
    small_ids = np.asarray(inputs["ids"]).T[SMALL]
    args = dict(small_ids=given("small_ids", small_ids), dense=given("dense", inputs["dense_ctx"]), ids=given("ids", inputs["ids"]),
                w1_rows=given("w1_rows", rows), tables=tables)
    for short, name in (("w1", "W_top1"), ("w2", "W_top2")):
        args[short] = given(short, inputs[name])
    for short, name in (("b1", "b_top1"), ("b2", "b_top2"), ("w3", "W_top3")):
        args[short] = given(short, np.asarray(inputs[name]).reshape(-1, P).T)
    out = nc.dram_tensor("y_out", (B, 1), F32, kind="ExternalOutput").ap()
    dlrm_tower(nc, out=out, **args)
    r = run_bass_kernel_spmd(nc, [arrays], core_ids=[0])
    return r.results[0]["y_out"]
```

```python
from contextlib import ExitStack

import concourse.bass as bass
from concourse import mybir

P = 128
B, F, D = 2048, 32, 16
N_DENSE, H1, H2 = 16, 512, 256
N_PAIRS = F * (F - 1) // 2
TILES = B // P
HALF_TILES = TILES // 2
WRAP = F // 2
CHUNK = P // F
CHUNKS = (N_PAIRS + N_DENSE) // P
LAST = N_PAIRS - (CHUNKS - 1) * P

F32 = mybir.dt.float32
BF16 = mybir.dt.bfloat16
F16 = mybir.dt.float16
I32 = mybir.dt.int32
ALU = mybir.AluOpType
ACT = mybir.ActivationFunctionType
AX = mybir.AxisListType

VOCABS = [12500, 1000, 1250, 1000, 1000, 12500, 1250, 125000, 125000, 12500, 12500, 1000, 1250, 125000, 1250, 125000,
          1250, 125000, 1000, 1250, 1250, 1250, 1250, 1000, 1000, 1250, 12500, 125000, 12500, 125000, 125000, 125000]
SMALL = [f for f in range(F) if VOCABS[f] == 1250] + [f for f in range(F) if VOCABS[f] == 1000]
LARGE = [f for f in range(F) if f not in SMALL]
FIELDS = SMALL + LARGE
BUNDLES = [[WRAP]] + [list(range(i, i + 4)) for i in range(0, WRAP, 4)]
ALONE, FOUR = 0, 1
KIND = [FOUR if len(b) > 1 else ALONE for b in BUNDLES]
CANDS = [P // (len(b) * D) for b in BUNDLES]
WIDTH = [c * D for c in CANDS]
ROWS = 125
SLICES = [max(VOCABS[SMALL[i]] for i in b) // (c * ROWS) for b, c in zip(BUNDLES, CANDS)]
SHORT = [i for b, c, n in zip(BUNDLES, CANDS, SLICES) for i in b if VOCABS[SMALL[i]] < c * n * ROWS]
SHORT_BLOCK = 96
PARTS = 3
MOST = max(n * w for n, w in zip(SLICES, WIDTH))
HB = B // 2
UNITS = 2 * len(BUNDLES)
RING = 5
ID_PLACES = 3
IDS_PER_P = WRAP * B // P
WARM_UP = (22, 16)

def mlp_input_rows():
    rows = []
    for k in range(1, F // 2 + 1):
        for i in range(F if k < F // 2 else F // 2):
            a, b = sorted((FIELDS[i], FIELDS[(i + k) % F]))
            rows.append(a * (2 * F - a - 1) // 2 + b - a - 1)
    return rows + list(range(N_PAIRS, N_PAIRS + N_DENSE))


def dlrm_tower(nc, dense, ids, small_ids, ids_dram, tables, w1, b1, w2, b2, w3, out):
    with ExitStack() as ctx:
        def sb(name, shape, dt=F32):
            return ctx.enter_context(nc.sbuf_tensor(name, shape, dt))

        def sem(name):
            return ctx.enter_context(nc.semaphore(name))

        emb = sb("emb", [P, TILES, (F + WRAP) * D])
        idx = sb("idx", [P, TILES, F], I32)
        tab = sb("tab", [ROWS, len(SMALL), MOST])
        parts = sb("parts", [ROWS, 2, 4, PARTS, MOST], BF16)
        group_of_int = sb("group_of_int", [ROWS, len(BUNDLES), max(SLICES)], I32)
        group_of = sb("group_of", [ROWS, len(BUNDLES), max(SLICES)])
        cand_int = sb("cand_int", [P, 3], I32)
        cand_of = sb("cand_of", [P, 2])
        ids_flat = [sb("id_alone", [P, B // P], I32), sb("ids_of_four", [P, IDS_PER_P], I32)]
        ids_int = [sb("int_alone", [P, 2, B // P], I32), sb("ints_of_four", [P, 2, IDS_PER_P], I32)]
        ids_f16 = [sb("f16_alone", [P, 2, B // P], F16), sb("f16_of_four", [P, 2, IDS_PER_P], F16)]
        group_ids = sb("group_ids", [P, ID_PLACES, 4, HB], F16)
        cand_ids = sb("cand_ids", [P, 2, B], F16)
        onehot = sb("onehot", [ROWS, RING, 4, HB], BF16)
        prod = sb("prod", [P, CHUNKS, P * D])
        picked = prod[:, 2, :]
        z_last = sb("z_last", [P, 2, P])
        z_end = sb("z_end", [P, 2, P])
        zT = sb("zT", [P, 2, CHUNKS, P])
        h1T = sb("h1T", [P, H1 // P, P])
        h2T = sb("h2T", [P, H2 // P, P])
        y = sb("y", [1, B])
        w1_sb = sb("w1_sb", [P, CHUNKS, H1])
        w2_sb = sb("w2_sb", [P, H1 // P, H2])
        w3_sb = sb("w3_sb", [P, H2 // P])
        b1_sb = sb("b1_sb", [P, H1 // P])
        b2_sb = sb("b2_sb", [P, H2 // P])
        ident = sb("ident", [P, P])
        bank = ctx.enter_context(nc.psum_tensor("bank", [P, 8, 512], F32))
        Z_BANK, H1_BANK, H2_BANK, Y_BANK = 0, 2, 4, 6
        END_ORDER, END_BANK = (0, 3, 2, 1), (1, 0, 1, 7)
        LOOK_BANK, TURN_BANK = 2, 6

        ids_loaded = sem("ids_loaded")
        w_loaded = sem("w_loaded")
        dense_loaded = [sem(f"dense_loaded{i}") for i in range(2)]
        ident_zeroed = sem("ident_zeroed")
        ident_ready = sem("ident_ready")
        iotas_made = sem("iotas_made")
        cand_steps = sem("cand_steps")
        tab_zeroed = sem("tab_zeroed")
        tab_loaded = [sem(f"tab_loaded{i}") for i in range(3)]
        ids_loaded_flat = [sem(f"ids_flat_loaded{i}") for i in range(2)]
        ids_split = sem("ids_split")
        ids_converted = sem("ids_converted")
        ids_stored = [sem(f"ids_stored{i}") for i in range(2)]
        groups_loaded = [sem(f"groups_loaded{i}") for i in range(ID_PLACES)]
        cands_loaded = [sem(f"cands_loaded{i}") for i in range(2)]
        first_part = sem("first_part")
        second_part = sem("second_part")
        rests = sem("rests")
        onehot_made = sem("onehot_made")
        looked = sem("looked")
        selected = sem("selected")
        turned_cands = sem("turned_cands")
        first_cands = sem("first_cands")
        in_emb = sem("in_emb")
        repeated = sem("repeated")
        gathered = [sem(f"gathered{i}") for i in range(2)]
        prod_ready = sem("prod_ready")
        turned = sem("turned")
        last_prod = sem("last_prod")
        first_last = sem("first_last")
        first_turned = sem("first_turned")
        z_last_ready = sem("z_last_ready")
        dense_placed = sem("dense_placed")
        z_end_ready = sem("z_end_ready")
        end_prod = sem("end_prod")
        end_made = sem("end_made")
        end_turned = sem("end_turned")
        end_copied = sem("end_copied")
        z_copied = sem("z_copied")
        h1_ready = sem("h1_ready")
        h1_done = sem("h1_done")
        h2_ready = sem("h2_ready")
        h2_done = sem("h2_done")
        y_ready = sem("y_ready")
        y_copied = sem("y_copied")
        stored = sem("stored")

        dense_v = dense.rearrange("(t p) m -> p t m", p=P)

        def slices_before(u):
            return sum(SLICES[v // 2] for v in range(u))

        def look_bank(u):
            return Z_BANK if u == 0 else LOOK_BANK + 2 * (u % 2)

        def turn_bank(u):
            return Z_BANK if u == 1 else TURN_BANK

        def emb_of(u, pos):
            h, n = u % 2, len(BUNDLES[u // 2]) * D
            return emb[:, h * HALF_TILES:(h + 1) * HALF_TILES, pos * D:pos * D + n]

        def end_chunk(c):
            return bank[:, END_BANK[c], c * P:(c + 1) * P]

        def turned_cand(u):
            q = u // 2
            return bank[:, turn_bank(u):turn_bank(u) + 2, :].rearrange(
                "p a (t i c d) -> p (a t) i c d", i=len(BUNDLES[q]), c=CANDS[q], d=D)

        def tile_turned(t):
            return (CHUNKS - 1) * (t + 2)

        block = ctx.enter_context(nc.Block())

        def tables_of(q):
            return tab[:, BUNDLES[q][0]:BUNDLES[q][-1] + 1, 0:SLICES[q] * WIDTH[q]]

        def part_of(q, k):
            return parts[:, q % 2, 0:len(BUNDLES[q]), k, 0:SLICES[q] * WIDTH[q]]

        def load_tables(eng, q, loaded):
            for i in BUNDLES[q]:
                x = SLICES[q] * CANDS[q]
                rows = VOCABS[SMALL[i]] // x
                eng.dma_start(tab[0:rows, i, 0:x * D], tables[SMALL[i]].rearrange("(p x) d -> p (x d)", x=x)
                              ).then_inc(loaded, 16)

        @block.sync
        def _(sp):
            flat_ids = small_ids.rearrange("f b -> (f b)")
            for kind, part in ((ALONE, flat_ids[WRAP * B:]), (FOUR, flat_ids[0:WRAP * B])):
                sp.dma_start(ids_flat[kind][:], part.rearrange("(p n) -> p n", p=P)).then_inc(ids_loaded_flat[kind], 16)
            load_tables(sp, 1, tab_loaded[1])

            def store_ids(kind):
                for k in range(2):
                    fields = ids_dram[k, WRAP:WRAP + 1, :] if kind == ALONE else ids_dram[k, 0:WRAP, :]
                    sp.dma_start(fields.rearrange("f b -> (f b)").rearrange("(p n) -> p n", p=P),
                                 ids_f16[kind][:, k, :]).then_inc(ids_stored[kind], 16)

            def load_groups(u):
                b = BUNDLES[u // 2]
                h = u % 2
                sp.dma_start(group_ids[:, u % ID_PLACES, 0:len(b), :],
                             ids_dram[0:1, b[0]:b[-1] + 1, h * HB:(h + 1) * HB].to_broadcast([P, len(b), HB])
                             ).then_inc(groups_loaded[u % ID_PLACES], 16)

            def load_cands(q):
                for k, i in enumerate(BUNDLES[q]):
                    sp.dma_start(cand_ids[k * WIDTH[q]:(k + 1) * WIDTH[q], q % 2, :],
                                 ids_dram[1, i:i + 1, :].to_broadcast([WIDTH[q], B])
                                 ).then_inc(cands_loaded[q % 2], 16)

            sp.wait_ge(ids_converted, 1)
            store_ids(ALONE)
            sp.wait_ge(ids_converted, 2)
            store_ids(FOUR)
            sp.wait_ge(ids_stored[ALONE], 32)
            load_groups(0)
            load_groups(1)
            sp.wait_ge(ids_stored[FOUR], 32)
            load_groups(2)
            load_cands(0)
            sp.wait_ge(tab_zeroed, 1)
            load_tables(sp, 2, tab_loaded[2])
            sp.wait_ge(onehot_made, slices_before(1))
            load_groups(3)
            load_cands(1)
            for q in range(3, len(BUNDLES)):
                load_tables(sp, q, tab_loaded[2])
            sp.dma_start(w1_sb[:], w1.rearrange("(c p) n -> p c n", p=P)).then_inc(w_loaded, 16)
            for t in range(2):
                sp.dma_start(z_last[:, t, LAST:P], dense_v[:, t, :]).then_inc(dense_loaded[t], 16)
            sp.dma_start(w2_sb[:], w2.rearrange("(c p) n -> p c n", p=P)).then_inc(w_loaded, 16)
            sp.dma_start(w3_sb[:], w3).then_inc(w_loaded, 16)
            sp.dma_start(b1_sb[:], b1).then_inc(w_loaded, 16)
            sp.dma_start(b2_sb[:], b2).then_inc(w_loaded, 16)
            for u in range(4, UNITS):
                sp.wait_ge(onehot_made, slices_before(u - ID_PLACES + 1))
                load_groups(u)
                if u % 2 == 0:
                    sp.wait_ge(selected, u - 2)
                    load_cands(u // 2)
            with sp.Fori(1, TILES // 2) as j:
                for s in range(2):
                    sp.wait_ge(turned, tile_turned(2 * j + s - 2))
                    sp.dma_start(z_last[:, s, LAST:P], dense_v[:, bass.ds(2 * j + s, 1), :]
                                 ).then_inc(dense_loaded[s], 16)
            sp.wait_ge(y_copied, TILES)
            sp.dma_start(out.rearrange("b o -> o b"), y[:]).then_inc(stored, 16)
            sp.wait_ge(stored, 16)

        @block.gpsimd
        def _(pool):
            nc.gpsimd.memset(ident[:], 0.0).then_inc(ident_zeroed, 1)
            pool.wait_ge(ident_zeroed, 1)
            nc.gpsimd.affine_select(out=ident[:], in_=ident[:], compare_op=ALU.not_equal, fill=1.0, base=0,
                                    pattern=[[-1, P]], channel_multiplier=1).then_inc(ident_ready, 1)
            for q, n in enumerate(SLICES):
                nc.gpsimd.iota(group_of_int[:, q, :], pattern=[[1, max(SLICES)]], base=0, channel_multiplier=n
                               ).then_inc(iotas_made, 1)
            nc.gpsimd.iota(cand_int[:, 0:1], pattern=[[1, 1]], base=0, channel_multiplier=1).then_inc(iotas_made, 1)

            def gather(t):
                s = t % 2
                if t >= 2:
                    pool.wait_ge(gathered[s], t // 2 * 16 * len(LARGE))
                for pos, f in enumerate(LARGE, len(SMALL)):
                    nc.gpsimd.indirect_dma_start(
                        emb[:, t, pos * D:(pos + 1) * D], None, tables[f],
                        bass.IndirectOffsetOnAxis(ap=idx[:, t, f:f + 1], axis=0)).then_inc(gathered[s], 16)

            pool.wait_ge(ids_loaded, 16)
            for t in range(TILES):
                gather(t)

        @block.vector
        def _(dve):
            nc.vector.memset(y[:, 1:2], 0.0).then_inc(turned, CHUNKS - 1)
            nc.vector.memset(y[:, 2:3], 0.0).then_inc(z_copied, 2)
            nc.vector.memset(y[:, 3:4], 0.0).then_inc(h1_done, 2)

            nc.vector.memset(tab[SHORT_BLOCK:ROWS, SHORT[0]:SHORT[-1] + 1, :], 0.0).then_inc(tab_zeroed, 1)
            dve.wait_ge(iotas_made, len(BUNDLES) + 1)
            nc.vector.tensor_copy(group_of[:], group_of_int[:]).then_inc(cand_steps, 1)
            for kind in (ALONE, FOUR):
                nc.vector.tensor_scalar(cand_int[:, kind + 1:kind + 2], cand_int[:, 0:1], D.bit_length() - 1,
                                        CANDS[kind] - 1, ALU.logical_shift_right, ALU.bitwise_and
                                        ).then_inc(cand_steps, 1)
            dve.wait_ge(cand_steps, 3)
            nc.vector.tensor_copy(cand_of[:], cand_int[:, 1:3]).then_inc(cand_steps, 1)
            for kind in (ALONE, FOUR):
                dve.wait_ge(ids_loaded_flat[kind], 16)
                nc.vector.tensor_scalar(ids_int[kind][:, 0, :], ids_flat[kind][:], CANDS[kind].bit_length() - 1, None,
                                        ALU.logical_shift_right).then_inc(ids_split, 1)
                nc.vector.tensor_scalar(ids_int[kind][:, 1, :], ids_flat[kind][:], CANDS[kind] - 1, None,
                                        ALU.bitwise_and).then_inc(ids_split, 1)
                dve.wait_ge(ids_split, 2 * kind + 2)
                nc.vector.tensor_copy(ids_f16[kind][:], ids_int[kind][:]).then_inc(ids_converted, 1)

            def rest_after_first(q):
                dve.wait_ge(first_part, q + 1)
                nc.vector.tensor_tensor(tables_of(q), tables_of(q), part_of(q, 0), ALU.subtract).then_inc(rests, 1)

            def third_part(q):
                dve.wait_ge(second_part, q + 1)
                nc.vector.tensor_tensor(part_of(q, 2), tables_of(q), part_of(q, 1), ALU.subtract).then_inc(rests, 1)

            def onehot_of(u, s):
                q = u // 2
                n = slices_before(u) + s
                if n >= RING:
                    dve.wait_ge(looked, n - RING + 1)
                nc.vector.tensor_scalar(onehot[:, n % RING, 0:len(BUNDLES[q]), :],
                                        group_ids[0:ROWS, u % ID_PLACES, 0:len(BUNDLES[q]), :],
                                        group_of[:, q, s:s + 1], None, ALU.is_equal).then_inc(onehot_made, 1)

            def select(u):
                q, h = u // 2, u % 2
                if q > 0:
                    dve.wait_ge(turned_cands, u - 1)
                dve.wait_ge(cands_loaded[q % 2], 16 * sum(len(b) for b in BUNDLES[q % 2:q + 1:2]))
                dve.wait_ge(looked, slices_before(u + 1))
                nc.vector.scalar_tensor_tensor(
                    out=picked[:, h * HB:(h + 1) * HB].rearrange("p (g b) -> p g b", g=2),
                    in0=cand_ids[:, q % 2, h * HB:(h + 1) * HB].rearrange("p (g b) -> p g b", g=2),
                    scalar=cand_of[:, KIND[q]:KIND[q] + 1],
                    in1=bank[:, look_bank(u):look_bank(u) + 2, :],
                    op0=ALU.is_equal, op1=ALU.mult).then_inc(selected, 1)

            def add_candidates(u):
                q = u // 2
                if KIND[q] == FOUR:
                    dve.wait_ge(first_cands, u - 1)
                    e = emb_of(u, BUNDLES[q][0]).rearrange("p t (i d) -> p t i d", d=D)
                    nc.vector.tensor_tensor(e, e, turned_cand(u)[:, :, :, 1, :], ALU.add).then_inc(in_emb, 1)
                else:
                    dve.wait_ge(turned_cands, u + 1)
                    nc.vector.tensor_reduce(emb_of(u, BUNDLES[q][0]), turned_cand(u)[:, :, 0, :, :].rearrange("p t c d -> p t d c"),
                                            AX.X, ALU.add).then_inc(in_emb, 1)

            for q in range(2):
                rest_after_first(q)
                third_part(q)
            dve.wait_ge(cand_steps, 4)
            for u in range(UNITS):
                dve.wait_ge(groups_loaded[u % ID_PLACES], 16 * (u // ID_PLACES + 1))
                n = SLICES[u // 2]
                for s in range(n):
                    if u == 3 and s in (1, 2):
                        add_candidates(s - 1)
                    if u > 3 and s == 3:
                        add_candidates(u - 2)
                    if u > 2 and s == n - 1:
                        select(u - 1)
                    if u == 2 and s >= n - 2:
                        select(s - (n - 2))
                    onehot_of(u, s)
                    if u > 2 and u % 2 == 1 and u // 2 + 1 < len(BUNDLES):
                        if s == 1:
                            rest_after_first(u // 2 + 1)
                        if s == 3:
                            third_part(u // 2 + 1)

            def products(t, c):
                k0 = 1 + c * CHUNK
                ks = CHUNK if c < CHUNKS - 1 else CHUNK - 1
                e = emb[:, bass.ds(t, 1), 0:F * D].to_broadcast([P, ks, F * D])
                w = emb[:, bass.ds(t, 1), k0 * D:(k0 + F) * D].to_broadcast([P, ks, F * D])
                shifted = bass.AP(tensor=w.tensor, offset=w.offset, ap=[w.ap[0], [D, ks], w.ap[2]])
                return nc.vector.tensor_tensor(
                    prod[:, c, 0:ks * F * D].rearrange("p (k x) -> p k x", k=ks), e, shifted, ALU.mult)

            def last_products(t):
                products(t, CHUNKS - 1)
                half_way = (CHUNK - 1) * F * D
                return nc.vector.tensor_tensor(
                    prod[:, CHUNKS - 1, half_way:LAST * D],
                    emb[:, bass.ds(t, 1), 0:F * D // 2].rearrange("p a x -> p (a x)"),
                    emb[:, bass.ds(t, 1), F * D // 2:F * D].rearrange("p a x -> p (a x)"), ALU.mult)

            def sum_of(out, c, pairs):
                return nc.vector.tensor_reduce(out, prod[:, c, 0:pairs * D].rearrange("p (a d) -> p a d", d=D),
                                               AX.X, ALU.add)

            def tile(t, place, lands, end=None):
                dve.wait_ge(gathered[place], lands * 16 * len(LARGE))
                last_products(t).then_inc(last_prod, 1)
                dve.wait_ge(turned, 3 * t + 1)
                products(t, 0).then_inc(prod_ready, 1)
                dve.wait_ge(last_prod, t)
                sum_of(z_last[:, place, 0:LAST], CHUNKS - 1, LAST).then_inc(z_last_ready, 1)
                for c in (1, 2):
                    dve.wait_ge(turned, 3 * t + c + 1)
                    products(t, c).then_inc(end_prod if end is not None and c == 2 else prod_ready, 1)
                if end is not None:
                    dve.wait_ge(end_prod, end + 1)
                    sum_of(z_end[:, end, :], 2, P).then_inc(z_end_ready, 1)
                dve.wait_ge(z_last_ready, t)

            dve.wait_ge(dense_loaded[0], 16)
            dense_pairs = prod[:, CHUNKS - 1, :].rearrange("p (a d) -> p a d", d=D)[:, LAST:P, 0]
            nc.vector.tensor_copy(dense_pairs, z_last[:, 0, LAST:P]).then_inc(dense_placed, 1)
            add_candidates(UNITS - 2)
            dve.wait_ge(in_emb, UNITS - 1)
            dve.wait_ge(repeated, UNITS - 1 - 2)
            dve.wait_ge(gathered[0], 16 * len(LARGE))
            last_products(0).then_inc(first_last, 1)
            select(UNITS - 1)
            products(0, 0).then_inc(prod_ready, 1)
            products(0, 1).then_inc(prod_ready, 1)
            add_candidates(UNITS - 1)
            products(0, 2).then_inc(prod_ready, 1)
            dve.wait_ge(in_emb, UNITS)
            dve.wait_ge(repeated, UNITS - 2)
            dve.wait_ge(first_turned, 1)
            with dve.Fori(0, TILES // 2 - 2) as j:
                tile(2 * j + 1, 1, j + 1)
                tile(2 * j + 2, 0, j + 2)
            tile(TILES - 3, 1, TILES // 2 - 1, end=0)
            tile(TILES - 2, 0, TILES // 2, end=1)
            t = TILES - 1
            dve.wait_ge(gathered[1], TILES // 2 * 16 * len(LARGE))
            dve.wait_ge(turned, 3 * t + 1)
            products(t, 0).then_inc(end_made, 1)
            last_products(t).then_inc(last_prod, 1)
            dve.wait_ge(turned, 3 * t + 2)
            products(t, 1).then_inc(end_prod, 1)
            dve.wait_ge(last_prod, t)
            sum_of(z_last[:, 1, 0:LAST], CHUNKS - 1, LAST).then_inc(z_last_ready, 1)
            dve.wait_ge(z_end_ready, 2)
            products(t, 2).then_inc(end_made, 1)
            dve.wait_ge(end_prod, 3)
            dve.wait_ge(turned, 3 * t)
            sum_of(z_end[:, 0, :], 1, P).then_inc(z_end_ready, 1)

        @block.tensor
        def _(pe):
            def sum_chunk(t, s, c, others=0):
                pe.wait_ge(prod_ready, 3 * t + c + 1 - others)
                v = prod[:, c, :].rearrange("p (a d) -> p d a", d=D)
                for d in range(D):
                    mm = nc.tensor.matmul(bank[:, Z_BANK + s % 2, c * P:(c + 1) * P], v[:, d, :], ident[:],
                                          start=(d == 0), stop=(d == D - 1), is_transpose=True)
                mm.then_inc(turned, 1)

            def sum_first_last():
                pe.wait_ge(first_last, 1)
                pe.wait_ge(dense_placed, 1)
                v = prod[:, CHUNKS - 1, :].rearrange("p (a d) -> p d a", d=D)
                for d in range(D):
                    n = P if d == 0 else LAST
                    mm = nc.tensor.matmul(bank[0:n, Z_BANK, (CHUNKS - 1) * P:], v[:, d, 0:n], ident[:],
                                          start=(d == 0), stop=(d == D - 1), is_transpose=True)
                mm.then_inc(first_turned, 1)

            def last_tile():
                t = TILES - 1
                pe.wait_ge(z_copied, t + 2)
                for n in range(H1 // P):
                    layer1(t - 1, 0, n)
                layer2(t - 1, 0)
                layer2(t - 1, 1)
                layer3(t - 1)
                pe.wait_ge(h1_done, 4 * t + 2)
                pe.wait_ge(h2_done, 2 * t)

                def sum_end(c, made):
                    pe.wait_ge(end_made, made)
                    v = prod[:, c, :].rearrange("p (a d) -> p d a", d=D)
                    for d in range(D):
                        mm = nc.tensor.matmul(end_chunk(c), v[:, d, :], ident[:],
                                              start=(d == 0), stop=(d == D - 1), is_transpose=True)
                    mm.then_inc(end_turned, 1)

                def add_chunk(c):
                    pe.wait_ge(end_copied, END_ORDER.index(c) + 1)
                    for n in range(H1 // P):
                        mm = nc.tensor.matmul(bank[:, H1_BANK + n, 0:P], w1_sb[:, c, n * P:(n + 1) * P],
                                              zT[:, 1, c, :], start=(c == END_ORDER[0]), stop=(c == END_ORDER[-1]))
                        if c == END_ORDER[-1]:
                            mm.then_inc(h1_ready, 1)

                sum_end(0, 1)
                pe.wait_ge(z_last_ready, t)
                pe.wait_ge(dense_loaded[1], 16 * HALF_TILES)
                nc.tensor.matmul(end_chunk(3), z_last[:, 1, :], ident[:],
                                 start=True, stop=True, is_transpose=True).then_inc(end_turned, 1)
                add_chunk(0)
                sum_end(2, 2)
                pe.wait_ge(z_end_ready, 3)
                nc.tensor.matmul(end_chunk(1), z_end[:, 0, :], ident[:],
                                 start=True, stop=True, is_transpose=True).then_inc(end_turned, 1)
                add_chunk(3)
                add_chunk(2)
                add_chunk(1)
                for c in range(H1 // P):
                    pe.wait_ge(h1_done, 4 * t + 2 + c + 1)
                    for m in range(H2 // P):
                        mm = nc.tensor.matmul(bank[:, Z_BANK + m, 0:P], w2_sb[:, c, m * P:(m + 1) * P],
                                              h1T[:, c, :], start=(c == 0), stop=(c == H1 // P - 1))
                        if c == H1 // P - 1:
                            mm.then_inc(h2_ready, 1)
                for c in range(H2 // P):
                    pe.wait_ge(h2_done, 2 * t + c + 1)
                    mm = nc.tensor.matmul(bank[0:1, Y_BANK, 0:P], w3_sb[:, c:c + 1],
                                          h2T[:, c, :], start=(c == 0), stop=(c == H2 // P - 1))
                mm.then_inc(y_ready, 1)

            def turn_last(t, s):
                pe.wait_ge(z_last_ready, t)
                pe.wait_ge(dense_loaded[s % 2], (t - s % 2) * 8 + 16)
                c = CHUNKS - 1
                return nc.tensor.matmul(bank[:, Z_BANK + s % 2, c * P:(c + 1) * P], z_last[:, s % 2, :], ident[:],
                                        start=True, stop=True, is_transpose=True)

            def layer1(t, place, n):
                pe.wait_ge(h1_done, 4 * t + n + 1)
                for c in range(CHUNKS):
                    mm = nc.tensor.matmul(bank[:, H1_BANK + n % 2, 0:P], w1_sb[:, c, n * P:(n + 1) * P],
                                          zT[:, place, c, :], start=(c == 0), stop=(c == CHUNKS - 1))
                mm.then_inc(h1_ready, 1)

            def layer2(t, m):
                if m == 0:
                    pe.wait_ge(h1_done, 4 * t + 4 + 2)
                for c in range(H1 // P):
                    mm = nc.tensor.matmul(bank[:, H2_BANK + m, 0:P], w2_sb[:, c, m * P:(m + 1) * P],
                                          h1T[:, c, :], start=(c == 0), stop=(c == H1 // P - 1))
                mm.then_inc(h2_ready, 1)

            def layer3(t):
                pe.wait_ge(h2_done, 2 * t + 2)
                for c in range(H2 // P):
                    mm = nc.tensor.matmul(bank[0:1, Y_BANK, 0:P], w3_sb[:, c:c + 1],
                                          h2T[:, c, :], start=(c == 0), stop=(c == H2 // P - 1))
                mm.then_inc(y_ready, 1)

            def tile(t, place, end=None):
                pe.wait_ge(z_copied, t + 1)
                sum_chunk(t, place, 0, end or 0)
                pe.wait_ge(z_copied, t + 2)
                layer1(t - 1, 1 - place, 0)
                layer1(t - 1, 1 - place, 1)
                turn_last(t, place)
                layer1(t - 1, 1 - place, 2)
                layer1(t - 1, 1 - place, 3)
                sum_chunk(t, place, 1, end or 0)
                layer2(t - 1, 0)
                layer2(t - 1, 1)
                if end is not None:
                    pe.wait_ge(z_end_ready, end + 1)
                    nc.tensor.matmul(bank[:, Z_BANK + place, 2 * P:3 * P], z_end[:, end, :], ident[:],
                                     start=True, stop=True, is_transpose=True).then_inc(turned, 1)
                else:
                    sum_chunk(t, place, 2)
                layer3(t - 1)

            def look_up(u):
                q, h = u // 2, u % 2
                n = SLICES[q]
                between = {0: [], 1: [], 2: [0, 1]}.get(u, [u - 1])
                sums = [(v, t) for v in between for t in range(HALF_TILES)]
                step = 0
                pe.wait_ge(rests, 2 * q + 2)
                if u > 2:
                    pe.wait_ge(selected, u - 1)
                for s in range(n):
                    place = (slices_before(u) + s) % RING
                    pe.wait_ge(onehot_made, slices_before(u) + s + 1)
                    for k in range(PARTS):
                        for g in range(2):
                            for i in range(len(BUNDLES[q])):
                                mm = nc.tensor.matmul(
                                    bank[i * WIDTH[q]:(i + 1) * WIDTH[q], look_bank(u) + g, :],
                                    parts[:, q % 2, i, k, s * WIDTH[q]:(s + 1) * WIDTH[q]],
                                    onehot[:, place, i, g * 512:(g + 1) * 512],
                                    start=(s == 0 and k == 0), stop=(s == n - 1 and k == PARTS - 1))
                            if (k, g) == (PARTS - 1, 1):
                                mm.then_inc(looked, 1)
                            start = 20 if u == 3 else 9
                            if u == UNITS - 1:
                                due = sums if step == 4 else []
                            else:
                                due = sums[step - start:step - start + 1] if step >= start else []
                            for v, t in due:
                                turn_candidates(v, t)
                            step += 1

            def turn_candidates(u, t):
                if t == 0:
                    pe.wait_ge(selected, u + 1)
                    if u > 1:
                        pe.wait_ge(in_emb, u)
                mm = nc.tensor.matmul(bank[:, turn_bank(u) + t // 4, t % 4 * P:(t % 4 + 1) * P],
                                      picked[:, bass.ts(u % 2 * HALF_TILES + t, P)], ident[:],
                                      start=True, stop=True, is_transpose=True)
                if t == HALF_TILES - 1:
                    mm.then_inc(turned_cands, 1)

            def warm_up(times):
                for _ in range(times):
                    nc.tensor.matmul(bank[:, LOOK_BANK, 0:P], ident[:], ident[:], start=True, stop=True)

            pe.wait_ge(ident_ready, 1)
            warm_up(WARM_UP[0])
            look_up(0)
            look_up(1)
            warm_up(WARM_UP[1])
            for u in range(2, UNITS):
                look_up(u)

            sum_first_last()
            for t in range(HALF_TILES):
                turn_candidates(UNITS - 1, t)
            sum_chunk(0, 0, 0)
            sum_chunk(0, 0, 1)
            sum_chunk(0, 0, 2)
            pe.wait_ge(w_loaded, 80)
            with pe.Fori(0, TILES // 2 - 2) as j:
                tile(2 * j + 1, 1)
                tile(2 * j + 2, 0)
            tile(TILES - 3, 1, end=0)
            tile(TILES - 2, 0, end=1)
            last_tile()

        @block.scalar
        def _(act):
            def copy_z(t, place):
                act.wait_ge(turned, tile_turned(t))
                nc.scalar.copy(zT[:, place, :, :],
                               bank[:, Z_BANK + place, :].rearrange("p (c b) -> p c b", c=CHUNKS)
                               ).then_inc(z_copied, 1)

            def relu1(t, n):
                act.wait_ge(h1_ready, 4 * t + n + 1)
                nc.scalar.activation(h1T[:, n, :], bank[:, H1_BANK + n % 2, 0:P], ACT.Relu,
                                     bias=b1_sb[:, n:n + 1]).then_inc(h1_done, 1)

            def relu2(t, m):
                act.wait_ge(h2_ready, 2 * t + m + 1)
                nc.scalar.activation(h2T[:, m, :], bank[:, H2_BANK + m, 0:P], ACT.Relu,
                                     bias=b2_sb[:, m:m + 1]).then_inc(h2_done, 1)

            def copy_y(t):
                act.wait_ge(y_ready, t + 1)
                act.nop(nofuse=True)
                nc.scalar.copy(y[0:1, bass.ts(t, P)], bank[0:1, Y_BANK, 0:P]).then_inc(y_copied, 1)

            def tile(t, place):
                for n in range(H1 // P):
                    relu1(t - 1, n)
                for m in range(H2 // P):
                    relu2(t - 1, m)
                copy_z(t, place)
                copy_y(t - 1)

            def first(q):
                nc.scalar.copy(part_of(q, 0), tables_of(q)).then_inc(first_part, 1)

            def second(q):
                act.wait_ge(rests, 2 * q + 1)
                nc.scalar.copy(part_of(q, 1), tables_of(q)).then_inc(second_part, 1)

            def first_cand(u):
                act.wait_ge(turned_cands, u + 1)
                nc.scalar.copy(emb_of(u, BUNDLES[u // 2][0]).rearrange("p t (i d) -> p t i d", d=D),
                               turned_cand(u)[:, :, :, 0, :]).then_inc(first_cands, 1)

            def repeat(u):
                pos = BUNDLES[u // 2][0]
                act.wait_ge(in_emb, u + 1)
                nc.scalar.copy(emb_of(u, F + pos), emb_of(u, pos)).then_inc(repeated, 1)

            act.dma_start(idx[:], ids).then_inc(ids_loaded, 16)
            load_tables(act, 0, tab_loaded[0])
            act.wait_ge(tab_loaded[0], 16)
            first(0)
            second(0)
            act.wait_ge(tab_loaded[1], 16 * 4)
            first(1)
            second(1)
            for q in range(len(BUNDLES)):
                if q > 0:
                    first_cand(2 * q)
                    repeat(2 * q)
                if q + 2 < len(BUNDLES):
                    if q == 0:
                        act.wait_ge(tab_loaded[2], 16 * 12)
                    act.wait_ge(looked, slices_before(2 * q + 2))
                    first(q + 2)
                if q > 0:
                    first_cand(2 * q + 1)
                    repeat(2 * q + 1)
                if q + 2 < len(BUNDLES):
                    second(q + 2)

            act.wait_ge(w_loaded, 80)
            act.wait_ge(first_turned, 1)
            copy_z(0, 0)
            with act.Fori(0, TILES // 2 - 1) as j:
                tile(2 * j + 1, 1)
                tile(2 * j + 2, 0)
            t = TILES - 1
            for n in range(H1 // P):
                relu1(t - 1, n)
            for m in range(H2 // P):
                relu2(t - 1, m)
            copy_y(t - 1)
            for k, c in enumerate(END_ORDER):
                act.wait_ge(end_turned, k + 1)
                nc.scalar.copy(zT[:, 1, c, :], end_chunk(c)).then_inc(end_copied, 1)
            for n in range(H1 // P):
                act.wait_ge(h1_ready, 4 * t + n + 1)
                nc.scalar.activation(h1T[:, n, :], bank[:, H1_BANK + n, 0:P], ACT.Relu,
                                     bias=b1_sb[:, n:n + 1]).then_inc(h1_done, 1)
            for m in range(H2 // P):
                act.wait_ge(h2_ready, 2 * t + m + 1)
                nc.scalar.activation(h2T[:, m, :], bank[:, Z_BANK + m, 0:P], ACT.Relu,
                                     bias=b2_sb[:, m:m + 1]).then_inc(h2_done, 1)
            copy_y(t)


def kernel(**inputs):
    import numpy as np
    import concourse.bacc as bacc
    from concourse.bass_utils import run_bass_kernel_spmd

    nc = bacc.Bacc("TRN2", target_bir_lowering=False, num_devices=1)
    arrays = {}

    def given(name, a):
        a = np.ascontiguousarray(a)
        arrays[name] = a
        return nc.dram_tensor(name, a.shape, mybir.dt.from_np(a.dtype), kind="ExternalInput").ap()

    tables = [given(f"tbl_{f}", inputs[f"tbl_{f}"]) for f in range(F)]
    assert [inputs[f"tbl_{f}"].shape[0] for f in range(F)] == VOCABS
    small_ids = np.asarray(inputs["ids"]).T[SMALL]
    args = dict(small_ids=given("small_ids", small_ids), dense=given("dense", inputs["dense_ctx"]), ids=given("ids", np.asarray(inputs["ids"]).reshape(TILES, P, F).transpose(1, 0, 2)),
                tables=tables)
    args["w1"] = given("w1", np.asarray(inputs["W_top1"])[mlp_input_rows()])
    args["w2"] = given("w2", inputs["W_top2"])
    for short, name in (("b1", "b_top1"), ("b2", "b_top2"), ("w3", "W_top3")):
        args[short] = given(short, np.asarray(inputs[name]).reshape(-1, P).T)
    args["ids_dram"] = nc.dram_tensor("small_ids_f16", (2, len(SMALL), B), F16, kind="Internal").ap()
    out = nc.dram_tensor("y_out", (B, 1), F32, kind="ExternalOutput").ap()
    dlrm_tower(nc, out=out, **args)
    r = run_bass_kernel_spmd(nc, [arrays], core_ids=[0])
    return r.results[0]["y_out"]
```
